# Optimizing a Trainium2 kernel written in Bass

```python
import numpy as np
import jax
import jax.numpy as jnp

def _softmax(x, axis=-1):
    return jax.nn.softmax(x, axis=axis)

def _gelu(x):
    return jax.nn.gelu(x, approximate=True)

def _silu(x):
    return jax.nn.silu(x)

def _sigmoid(x):
    return jax.nn.sigmoid(x)

def _layernorm(x, axis=-1, eps=1e-05):
    m = jnp.mean(x, axis=axis, keepdims=True)
    v = jnp.var(x, axis=axis, keepdims=True)
    return (x - m) / jnp.sqrt(v + eps)

def _scatter_add(tgt, idx, src, axis=0):
    return tgt.at[idx].add(src)

def _segment_sum(src, seg, n):
    return jax.ops.segment_sum(src, seg, n)
kernel_name = 'mk_adj_preln_d2_adj_r2_321b0d'

def setup_inputs(seed: int=0):
    np.random.seed(seed)
    _w = jnp.asarray

    def _rec_inputs():
        import jax
        import jax.numpy as jnp
        _gk = jax.random.key(seed)
        x = -0.0002928 + 1 * jax.random.normal(jax.random.fold_in(_gk, 1), (8, 1024, 128), jnp.float32)
        _a = jax.random.bernoulli(jax.random.fold_in(_gk, 2), 0.015625, (8, 1024, 1024))
        adj = _a.astype(jnp.int32)
        return (x, adj)
    x, adj = _rec_inputs()

    def _L0_gnn_setup():
        import jax, jax.numpy as jnp
        import numpy as np
        IN_F = 128
        OUT_F = 128
        ALPHA = 0.2

        def _xavier(key, shape, gain=1.414):
            fan_in, fan_out = (shape[0], shape[1])
            limit = gain * np.sqrt(6.0 / (fan_in + fan_out))
            return jax.random.uniform(key, shape, jnp.float32, -limit, limit)
        key = jax.random.key(seed)
        k1, k2, k3, k4 = jax.random.split(key, 4)
        B, N = (8, 1024)
        h = jax.random.normal(k1, (B, N, IN_F), jnp.float32)
        adj = jax.random.randint(k2, (B, N, N), 0, 2, jnp.int32)
        W = _xavier(k3, (IN_F, OUT_F))
        a = _xavier(k4, (2 * OUT_F, 1))
        return {'h': h, 'adj': adj, 'W': W, 'a': a}
    _L0_gnn_all = _L0_gnn_setup()
    _L0_gnn_in = {k: v for k, v in _L0_gnn_all.items() if k in ('W', 'a')}
    del _L0_gnn_all

    def _L1_gnn_setup():
        import jax, jax.numpy as jnp
        import numpy as np
        NEG_INF = -1000000000.0
        LEAKY_SLOPE = 0.2
        key = jax.random.key(seed)
        k1, k2, k3, k4 = jax.random.split(key, 4)
        B, N, D_in, D_out = (8, 1024, 128, 128)
        x = jax.random.normal(k1, (B, N, D_in), dtype=jnp.float32)
        adj_matrix = jax.random.randint(k2, (B, N, N), 0, 2, dtype=jnp.int32)
        W = jax.random.normal(k3, (D_out, D_in), dtype=jnp.float32) / np.sqrt(D_in)
        a = jax.random.normal(k4, (1, 2 * D_out), dtype=jnp.float32) / np.sqrt(2 * D_out)
        return {'x': x, 'adj_matrix': adj_matrix, 'W': W, 'a': a}
    _L1_gnn_all = _L1_gnn_setup()
    _L1_gnn_in = {k: v for k, v in _L1_gnn_all.items() if k in ('W', 'a')}
    del _L1_gnn_all
    return {'x': x, 'adj': adj, 'L0_gnn_W': _L0_gnn_in['W'], 'L0_gnn_a': _L0_gnn_in['a'], 'L1_gnn_W': _L1_gnn_in['W'], 'L1_gnn_a': _L1_gnn_in['a']}

def reference(x, adj, L0_gnn_W, L0_gnn_a, L1_gnn_W, L1_gnn_a):
    import jax
    import jax.numpy as jnp

    def _L0_gnn_ref(h, adj, W, a):
        import jax, jax.numpy as jnp
        import numpy as np
        IN_F = 128
        OUT_F = 128
        ALPHA = 0.2

        def _xavier(key, shape, gain=1.414):
            fan_in, fan_out = (shape[0], shape[1])
            limit = gain * np.sqrt(6.0 / (fan_in + fan_out))
            return jax.random.uniform(key, shape, jnp.float32, -limit, limit)
        Wh = jnp.einsum('bni,io->bno', h, W)
        a1 = a[:OUT_F, 0]
        a2 = a[OUT_F:, 0]
        e1 = Wh @ a1
        e2 = Wh @ a2
        e = e1[:, :, None] + e2[:, None, :]
        e = jnp.where(e > 0, e, ALPHA * e)
        neg = jnp.float32(-9000000000000000.0)
        scores = jnp.where(adj > 0, e, neg)
        attention = jax.nn.softmax(scores, axis=2)
        h_prime = jnp.einsum('bnm,bmo->bno', attention, Wh)
        return jax.nn.elu(h_prime)

    def _L1_gnn_ref(x, adj_matrix, W, a):
        import jax, jax.numpy as jnp
        import numpy as np
        NEG_INF = -1000000000.0
        LEAKY_SLOPE = 0.2
        h = jnp.einsum('bnd,od->bno', x, W)
        D = h.shape[-1]
        a_left, a_right = (a[0, :D], a[0, D:])
        e = (h @ a_left)[:, :, None] + (h @ a_right)[:, None, :]
        e = jnp.where(e > 0, e, LEAKY_SLOPE * e)
        e = jnp.where(adj_matrix == 0, NEG_INF, e)
        alpha = jax.nn.softmax(e, axis=-1)
        return jnp.einsum('bij,bjd->bid', alpha, h)
    h = jnp.maximum(_layernorm(x, axis=-1), 0.0)
    x = x + _L0_gnn_ref(h, adj, L0_gnn_W, L0_gnn_a)
    h = jnp.maximum(_layernorm(x, axis=-1), 0.0)
    x = x + _L1_gnn_ref(h, adj, L1_gnn_W, L1_gnn_a)
    return x

_drawn_inputs = setup_inputs


def setup_inputs(seed=0):
    import zlib

    import numpy as np

    out = dict(_drawn_inputs(seed))
    spreads = {}
    factors = {}
    for name, (base, spread) in spreads.items():
        noise = np.random.default_rng([zlib.crc32(name.encode()), seed]).standard_normal(out[name].shape)
        drawn = base * np.exp(spread * noise) if base else spread * noise
        out[name] = jnp.asarray(drawn.astype(out[name].dtype))
    for name, factor in factors.items():
        out[name] = (out[name] * factor).astype(out[name].dtype)
    return out
```

```python
from contextlib import ExitStack

import concourse.bass as bass
from concourse import mybir

P = 128
F32 = mybir.dt.float32
I32 = mybir.dt.int32
ALU = mybir.AluOpType
ACT = mybir.ActivationFunctionType
AX_X = mybir.AxisListType.X

SLOPE = 0.2
EPS = 1e-5
EMPTY = 2.0 ** -110


def gat_two_layers(nc, x, adj, w0, w0t, a0, w1, w1t, a1, out):
    B, T, _, N = adj.shape
    D = x.shape[2]
    C = D + 1
    E = D + 2
    BANK = 512
    NB = 3
    LAST = 2 * B - 1
    BUFS = 4
    bank_of = [(i // NB, i % NB) for i in range(T)]
    tiles_in = [NB, NB, T - 2 * NB]

    xv = x.rearrange("b (p t) d -> b p (t d)", t=T)
    ov = out.rearrange("b (p t) d -> b p (t d)", t=T)

    with ExitStack() as ctx:
        def sb(name, shape, dt=F32):
            return ctx.enter_context(nc.sbuf_tensor(name, shape, dt))

        def ps(name, shape):
            return ctx.enter_context(nc.psum_tensor(name, shape, F32))

        def sem(name):
            return ctx.enter_context(nc.semaphore(name))

        ident = sb("ident", [P, P])
        neg_half = sb("neg_half", [P, T])
        neg_one = sb("neg_one", [P, 1])
        gate = sb("gate", [P, 1])
        w_ext = sb("w_ext", [P, 2, E])
        w_tr = sb("w_tr", [P, 2, D])
        a_cols = sb("a_cols", [P, 2, 2])
        adj_sb = sb("adj_sb", [P, 2 * T * N], I32)
        x0 = sb("x0", [P, 2 * T * D])
        x1 = sb("x1", [P, 2 * T * D])
        stats = sb("stats", [P, T, 6])
        mean2 = sb("mean2", [P, T])
        mdiff = sb("mdiff", [P, T])
        m2sum = sb("m2sum", [P, T])
        mean = sb("mean", [P, T])
        between = sb("between", [P, T])
        var = sb("var", [P, T])
        vareps = sb("vareps", [P, T])
        rstd = sb("rstd", [P, T])
        xn = sb("xn", [P, T, D])
        hT = sb("hT", [P, T * P])
        hsum = sb("hsum", [P, 1])
        wh = sb("wh", [P, 2, T, C])
        ecol = sb("ecol", [P, T, 2])
        emax = sb("emax", [P, 1])
        cmax = sb("cmax", [P, 1])
        zrow = sb("zrow", [P, T])
        args = sb("args", [P, 3, T])
        vqr = sb("vqr", [P, 2, 3, T])
        negv = sb("negv", [P, 2, T])
        row_r = sb("row_r", [P, 2, N])
        uniform = sb("uniform", [P, 2, C])
        fbuf = sb("fbuf", [P, BUFS, N])
        pbuf = sb("pbuf", [P, BUFS, N])
        accs = sb("accs", [P, T, C])
        rec = sb("rec", [P, T])
        hp = sb("hp", [P, T, D])
        x0m = sb("x0m", [P, T * D])
        ex = sb("ex", [P, T * D])
        outb = sb("outb", [P, T * D])

        acc = ps("acc", [P, NB, BANK])
        prj = ps("prj", [P, NB, BANK])
        tp = ps("tp", [P, 2 * BANK])
        USUM = prj[:, NB - 1, tiles_in[-1] * E:tiles_in[-1] * E + D]

        w_in = sem("w_in")
        x_in = sem("x_in")
        adj_in = [sem(f"adj_in{t}") for t in range(T)]
        const_set = sem("const_set")
        wa_done = sem("wa_done")
        wext_ready = sem("wext_ready")
        bn_done = sem("bn_done")
        halves_done = sem("halves_done")
        mean_ready = sem("mean_ready")
        var_done = sem("var_done")
        vareps_ready = sem("vareps_ready")
        rstd_ready = sem("rstd_ready")
        centred = sem("centred")
        xn_ready = sem("xn_ready")
        tr_done = sem("tr_done")
        hT_ready = sem("hT_ready")
        prj_done = sem("prj_done")
        e_copied = sem("e_copied")
        wh_ready = sem("wh_ready")
        emax_ready = sem("emax_ready")
        emax_spread = sem("emax_spread")
        cmax_ready = sem("cmax_ready")
        z_ready = sem("z_ready")
        args_ready = sem("args_ready")
        vqr_ready = sem("vqr_ready")
        negv_ready = sem("negv_ready")
        r_spread = sem("r_spread")
        row_ready = sem("row_ready")
        f_ready = sem("f_ready")
        p_ready = sem("p_ready")
        p_used = sem("p_used")
        acc_done = sem("acc_done")
        acc_copied = sem("acc_copied")
        rec_ready = sem("rec_ready")
        hp_ready = sem("hp_ready")
        x0m_ready = sem("x0m_ready")
        ex_ready = sem("ex_ready")
        elu_ready = sem("elu_ready")
        x1_ready = sem("x1_ready")
        out_ready = sem("out_ready")
        out_stored = sem("out_stored")

        def x_at(buf, b):
            return buf[:, bass.ds((b % 2) * (T * D), T * D)]

        def x3_at(buf, b):
            return x_at(buf, b).rearrange("p (t d) -> p t d", t=T)

        def schedule(eng, stage, peel_in, peel_out):
            def pair(k):
                stage(2 * k + 1, 1, 0, k + 1, (1, k - 1), 1, None, [(2 * k + 3, 0, k + 2)])
                stage(2 * k + 2, 0, 1, k, (0, k + 1), 0, None, [(2 * k + 4, 1, k + 1)])

            peel_in()
            stage(0, 0, 0, 0, None, 0, None, None)
            stage(1, 1, 0, 1, (0, 0), 1, [(2, 1, 0)], [(3, 0, 2)])
            stage(2, 0, 1, 0, (0, 1), 0, None, [(4, 1, 1)])
            pair(1)
            with eng.Fori(2, B - 2) as k:
                pair(k)
            stage(LAST - 2, 1, 0, B - 1, (1, B - 3), 1, None, None)
            stage(LAST - 1, 0, 1, B - 2, (0, B - 1), 1, [(LAST, 1, B - 1)], None)
            stage(LAST, 1, 1, B - 1, (1, B - 2), None, None, None)
            peel_out()

        block = ctx.enter_context(nc.Block())

        @block.sync
        def _(sp):
            def load_x(b):
                sp.dma_start(x_at(x0, b), xv[b]).then_inc(x_in, 16)

            def load_adj(b, t):
                sp.dma_start(adj_sb[:, bass.ds((b % 2) * (T * N) + t * N, N)],
                             adj[b, t]).then_inc(adj_in[t], 16)

            def store(b):
                sp.wait_ge(out_ready, b + 1)
                sp.dma_start(ov[b], outb[:, :]).then_inc(out_stored, 16)

            def later_loads(k):
                sp.wait_ge(x1_ready, k + 1)
                load_x(k + 2)

            def later_adj(k):
                for t in range(T):
                    sp.wait_ge(p_ready, 8 * (2 * k + 2) + t + 1)
                    load_adj(k + 2, t)

            load_x(0)
            for l, (w, wt, a) in enumerate(((w0, w0t, a0), (w1, w1t, a1))):
                sp.dma_start(w_tr[:, l, :], wt).then_inc(w_in, 16)
                sp.dma_start(a_cols[:, l, :], a).then_inc(w_in, 16)
                sp.dma_start(w_ext[:, l, 0:D], w).then_inc(w_in, 16)
            for t in range(T):
                load_adj(0, t)
            sp.wait_ge(x_in, 16)
            load_x(1)
            for t in range(T):
                sp.wait_ge(adj_in[t], 16)
                load_adj(1, t)
            later_loads(0)
            later_adj(0)
            with sp.Fori(1, B - 2) as k:
                later_loads(k)
                store(k - 1)
                later_adj(k)
            for b in range(B - 3, B):
                store(b)
            sp.wait_ge(out_stored, 16 * B)

        @block.gpsimd
        def _(pool):
            def normalise(m, l, b):
                pool.wait_ge(vareps_ready, m + 1)
                nc.gpsimd.tensor_tensor(rstd[:, :], vareps[:, :], neg_half[:, :],
                                        ALU.pow).then_inc(rstd_ready, 1)
                if not isinstance(m, int) or m > 0:
                    pool.wait_ge(tr_done, m)
                src = x3_at(x1 if l else x0, b)
                nc.gpsimd.tensor_tensor(xn[:, :, :], src,
                                        mean[:, :].unsqueeze(2).to_broadcast([P, T, D]),
                                        ALU.subtract).then_inc(centred, 1)
                pool.wait_ge(rstd_ready, m + 1)
                pool.wait_ge(centred, m + 1)
                nc.gpsimd.tensor_tensor(xn[:, :, :], xn[:, :, :],
                                        rstd[:, :].unsqueeze(2).to_broadcast([P, T, D]),
                                        ALU.mult).then_inc(xn_ready, 1)

            def epilogue(e, l, b):
                pool.wait_ge(rec_ready, e + 1)
                if l == 1:
                    pool.wait_ge(x1_ready, b + 2 if not isinstance(b, int) else min(b + 2, B))
                    if isinstance(b, int) and b == B - 1:
                        pool.wait_ge(out_ready, b)
                elif isinstance(b, int) and b == 1:
                    pool.wait_ge(x1_ready, 1)
                elif not isinstance(b, int) or b > 1:
                    pool.wait_ge(out_ready, b - 1)
                nc.gpsimd.tensor_tensor(hp[:, :, :], accs[:, :, 0:D],
                                        rec[:, :].unsqueeze(2).to_broadcast([P, T, D]),
                                        ALU.mult).then_inc(hp_ready, 1)
                if l == 0:
                    if not isinstance(b, int) or b > 0:
                        pool.wait_ge(elu_ready, b)
                    pool.wait_ge(x_in, 16 * (b + 1))
                    nc.gpsimd.tensor_tensor(x0m[:, :], x_at(x0, b),
                                            neg_one[:, 0:1].to_broadcast([P, T * D]),
                                            ALU.add).then_inc(x0m_ready, 1)
                else:
                    if not isinstance(b, int) or b > 0:
                        pool.wait_ge(out_stored, 16 * b)
                    pool.wait_ge(hp_ready, e + 1)
                    nc.gpsimd.tensor_tensor(outb[:, :], hp[:, :, :].rearrange("p t d -> p (t d)"),
                                            x_at(x1, b),
                                            ALU.add).then_inc(out_ready, 1)

            def setup():
                nc.gpsimd.memset(ident[:, :], 0.0).then_inc(const_set, 1)
                pool.wait_ge(const_set, 1)
                nc.gpsimd.affine_select(out=ident[:, :], in_=ident[:, :],
                                        compare_op=ALU.not_equal, fill=1.0, base=0,
                                        pattern=[[-1, P]], channel_multiplier=1).then_inc(const_set, 1)
                nc.gpsimd.memset(neg_half[:, :], -0.5).then_inc(const_set, 1)
                nc.gpsimd.memset(neg_one[:, :], -1.0).then_inc(const_set, 1)
                nc.gpsimd.memset(wh[:, :, :, D:C], 1.0).then_inc(const_set, 1)
                nc.gpsimd.memset(uniform[:, :, D:C], EMPTY * N).then_inc(const_set, 1)
                pool.wait_ge(const_set, 6)
                normalise(0, 0, 0)

            def stage(n, g, l, b, epi, prep, norm_now, norm_next):
                if epi is not None:
                    epilogue(n - 1, *epi)
                if isinstance(n, int) and n == 0:
                    normalise(1, 0, 1)
                for item in (norm_now or []) + (norm_next or []):
                    normalise(*item)

            def last():
                epilogue(LAST, 1, B - 1)

            schedule(pool, stage, setup, last)

        @block.scalar
        def _(act):
            def relu_hT(m):
                act.wait_ge(tr_done, m + 1)
                nc.scalar.activation(hT[:, :], tp[:, :], ACT.Relu,
                                     accum_out=hsum[:, :]).then_inc(hT_ready, 1)

            def copy_wh(m, g):
                act.wait_ge(e_copied, 3 * m + 3)
                full = prj[:, 0:2, 0:NB * E].rearrange("p b (s e) -> p b s e", e=E)[:, :, :, 0:D]
                nc.scalar.activation(
                    wh[:, g, 0:2 * NB, 0:D].rearrange("p (b s) d -> p b s d", b=2), full,
                    ACT.Copy).then_inc(wh_ready, 1)
                part = prj[:, 2, 0:tiles_in[2] * E].rearrange("p (s e) -> p s e", e=E)[:, :, 0:D]
                nc.scalar.activation(wh[:, g, 2 * NB:T, 0:D], part, ACT.Copy).then_inc(wh_ready, 1)

            def exps(m, g):
                act.wait_ge(args_ready, m + 1)
                nc.scalar.activation(vqr[:, g, :, :], args[:, :, :], ACT.Exp).then_inc(vqr_ready, 1)

            def copy_row(m, g):
                act.wait_ge(r_spread, m + 1)
                nc.scalar.activation(row_r[:, g, :], tp[:, :], ACT.Copy).then_inc(row_ready, 1)

            def f_tile(n, g, t):
                if t == 0:
                    act.wait_ge(negv_ready, n + 1)
                    act.wait_ge(row_ready, n + 1)
                if not (isinstance(n, int) and 8 * n + t < BUFS):
                    act.wait_ge(p_ready, 8 * n + t - BUFS + 1)
                nc.scalar.activation(fbuf[:, t % BUFS, :], row_r[:, g, :], ACT.Relu,
                                     bias=negv[:, g, t:t + 1],
                                     scale=vqr[:, g, 1, t:t + 1]).then_inc(f_ready, 1)

            def elu_exp(e, b):
                act.wait_ge(hp_ready, e + 1)
                if not isinstance(b, int) or b > 0:
                    act.wait_ge(elu_ready, b)
                nc.scalar.activation(ex[:, :], hp[:, :, :].rearrange("p t d -> p (t d)"),
                                     ACT.Exp).then_inc(ex_ready, 1)

            def prepare(m, g):
                relu_hT(m)
                copy_wh(m, g)
                exps(m, g)
                copy_row(m, g)

            def stage(n, g, l, b, epi, prep, norm_now, norm_next):
                elu = epi is not None and epi[0] == 0
                for t in range(T):
                    f_tile(n, g, t)
                    if elu and norm_now and t == 4:
                        elu_exp(n - 1, epi[1])
                    if not norm_now and t == 5:
                        if prep is not None:
                            relu_hT(n + 1)
                        if elu:
                            elu_exp(n - 1, epi[1])
                if norm_now:
                    relu_hT(n + 1)
                if prep is not None:
                    copy_wh(n + 1, 1 - g)
                    exps(n + 1, 1 - g)
                    copy_row(n + 1, 1 - g)

            schedule(act, stage, lambda: prepare(0, 0), lambda: None)

        @block.vector
        def _(dve):
            def statistics(m, l, b):
                if l:
                    dve.wait_ge(x1_ready, b + 1)
                else:
                    dve.wait_ge(x_in, 16 * (b + 1))
                nc.vector.memset(gate[:, :], 0.0)
                src = x3_at(x1 if l else x0, b)
                for t in range(T):
                    st = nc.vector.bn_stats(stats[:, t, :], src[:, t, :])
                st.then_inc(bn_done, 1)
                dve.wait_ge(bn_done, m + 1)
                if not isinstance(m, int) or m > 0:
                    dve.wait_ge(xn_ready, m)
                nc.vector.tensor_tensor(mean2[:, :], stats[:, :, 1], stats[:, :, 4],
                                        ALU.add).then_inc(halves_done, 1)
                nc.vector.tensor_tensor(mdiff[:, :], stats[:, :, 1], stats[:, :, 4],
                                        ALU.subtract).then_inc(halves_done, 1)
                nc.vector.tensor_tensor(m2sum[:, :], stats[:, :, 2], stats[:, :, 5],
                                        ALU.add).then_inc(halves_done, 1)
                dve.wait_ge(halves_done, 3 * m + 3)
                nc.vector.tensor_scalar(mean[:, :], mean2[:, :], 0.5, None,
                                        ALU.mult).then_inc(mean_ready, 1)
                nc.vector.scalar_tensor_tensor(between[:, :], mdiff[:, :], 0.25, mdiff[:, :],
                                               ALU.mult, ALU.mult).then_inc(mean_ready, 1)
                dve.wait_ge(mean_ready, 2 * m + 2)
                nc.vector.scalar_tensor_tensor(var[:, :], m2sum[:, :], 1.0 / D, between[:, :],
                                               ALU.mult, ALU.add).then_inc(var_done, 1)
                dve.wait_ge(var_done, m + 1)
                nc.vector.tensor_scalar(vareps[:, :], var[:, :], EPS, None,
                                        ALU.add).then_inc(vareps_ready, 1)

            def copy_e(m, g):
                dve.wait_ge(prj_done, m + 1)
                full = prj[:, 0:2, 0:NB * E].rearrange("p b (s e) -> p b s e", e=E)[:, :, :, D:E]
                nc.vector.tensor_copy(ecol[:, 0:2 * NB, :].rearrange("p (b s) e -> p b s e", b=2),
                                      full).then_inc(e_copied, 1)
                part = prj[:, 2, 0:tiles_in[2] * E].rearrange("p (s e) -> p s e", e=E)[:, :, D:E]
                nc.vector.tensor_copy(ecol[:, 2 * NB:T, :], part).then_inc(e_copied, 1)
                nc.vector.tensor_scalar(uniform[:, g, 0:D], USUM, EMPTY, None,
                                        ALU.mult).then_inc(e_copied, 1)
                dve.wait_ge(e_copied, 3 * m + 3)
                nc.vector.tensor_reduce(emax[:, :], ecol[:, :, 1], AX_X, ALU.max).then_inc(emax_ready, 1)

            def exp_args(m):
                dve.wait_ge(emax_spread, m + 1)
                nc.vector.tensor_reduce(cmax[:, :], tp[:, 0:P], AX_X, ALU.max).then_inc(cmax_ready, 1)
                dve.wait_ge(cmax_ready, m + 1)
                nc.vector.tensor_scalar(zrow[:, :], ecol[:, :, 0], cmax[:, 0:1], 0.0, ALU.add,
                                        ALU.max).then_inc(z_ready, 1)
                nc.vector.tensor_scalar(args[:, 0, :], ecol[:, :, 1], cmax[:, 0:1], None,
                                        ALU.subtract)
                nc.vector.tensor_scalar(args[:, 1, :], ecol[:, :, 1], cmax[:, 0:1], SLOPE,
                                        ALU.subtract, ALU.mult)
                dve.wait_ge(z_ready, m + 1)
                nc.vector.tensor_scalar(args[:, 2, :], zrow[:, :], SLOPE - 1.0, None,
                                        ALU.mult).then_inc(args_ready, 1)

            def negate_v(m, g):
                dve.wait_ge(vqr_ready, m + 1)
                nc.vector.tensor_scalar(negv[:, g, :], vqr[:, g, 0, :], -1.0, None,
                                        ALU.mult).then_inc(negv_ready, 1)

            def mask(n, g, l, b, t):
                dve.wait_ge(f_ready, 8 * n + t + 1)
                if l == 0:
                    dve.wait_ge(adj_in[t], 16 * (b + 1))
                if not (isinstance(n, int) and 8 * n + t < BUFS):
                    dve.wait_ge(p_used, 8 * n + t - BUFS + 1)
                nc.vector.scalar_tensor_tensor(
                    pbuf[:, t % BUFS, :], fbuf[:, t % BUFS, :], vqr[:, g, 0, t:t + 1],
                    adj_sb[:, bass.ds((b % 2) * (T * N) + t * N, N)],
                    ALU.add, ALU.min).then_inc(p_ready, 1)

            def copy_acc(e, g, k):
                if k == 0 and not (isinstance(e, int) and e == 0):
                    dve.wait_ge(hp_ready, e)
                if k < 2:
                    dve.wait_ge(acc_done, 2 * e + k + 1)
                else:
                    dve.wait_ge(p_used, 8 * e + 8)
                w = tiles_in[k]
                nc.vector.tensor_tensor(
                    accs[:, k * NB:k * NB + w, :],
                    acc[:, k, 0:w * C].rearrange("p (s c) -> p s c", c=C),
                    uniform[:, g, :].unsqueeze(1).to_broadcast([P, w, C]),
                    ALU.add).then_inc(acc_copied, 1)

            def take_acc(e, g):
                for k in range(NB):
                    copy_acc(e, g, k)
                dve.wait_ge(acc_copied, NB * e + NB)
                nc.vector.reciprocal(rec[:, :], accs[:, :, D]).then_inc(rec_ready, 1)

            def elu_half(b):
                dve.wait_ge(ex_ready, b + 1)
                dve.wait_ge(x0m_ready, b + 1)
                nc.vector.scalar_tensor_tensor(ex[:, :], ex[:, :], 1.0, x0m[:, :], ALU.min,
                                               ALU.add).then_inc(elu_ready, 1)

            def elu_rest(b):
                dve.wait_ge(elu_ready, b + 1)
                if not isinstance(b, int) or b > 1:
                    dve.wait_ge(out_ready, b - 1)
                nc.vector.scalar_tensor_tensor(
                    x_at(x1, b), hp[:, :, :].rearrange("p t d -> p (t d)"), 0.0, ex[:, :],
                    ALU.max, ALU.add).then_inc(x1_ready, 1)

            def elu_residual(b):
                elu_half(b)
                elu_rest(b)

            def prepare(m, g):
                copy_e(m, g)
                exp_args(m)
                negate_v(m, g)

            def setup():
                statistics(0, 0, 0)
                dve.wait_ge(wa_done, 1)
                nc.vector.tensor_copy(w_ext[:, :, D:E],
                                      prj[:, 0, 0:4].rearrange("p (l e) -> p l e", l=2)
                                      ).then_inc(wext_ready, 1)
                prepare(0, 0)
                statistics(1, 0, 1)

            def stage(n, g, l, b, epi, prep, norm_now, norm_next):
                elu = epi is not None and epi[0] == 0
                for t in range(T):
                    mask(n, g, l, b, t)
                    if epi is not None and t == 0:
                        take_acc(n - 1, 1 - g)
                    if norm_now:
                        if t == 4:
                            elu_residual(epi[1])
                            statistics(*norm_now[0])
                        continue
                    if elu and t == 4:
                        elu_half(epi[1])
                        if prep is not None:
                            copy_e(n + 1, 1 - g)
                        elu_rest(epi[1])
                        if prep is not None:
                            exp_args(n + 1)
                    if t == 5:
                        if prep is not None and not elu:
                            copy_e(n + 1, 1 - g)
                            exp_args(n + 1)
                        if prep is not None:
                            negate_v(n + 1, 1 - g)
                        if elu and norm_next:
                            statistics(*norm_next[0])
                    if t == 6 and norm_next and not elu:
                        statistics(*norm_next[0])
                if norm_now:
                    copy_e(n + 1, 1 - g)
                    exp_args(n + 1)
                    negate_v(n + 1, 1 - g)
                    if norm_next:
                        statistics(*norm_next[0])

            schedule(dve, stage, setup, lambda: take_acc(LAST, 1))

        @block.tensor
        def _(pe):
            def transposes(m):
                pe.wait_ge(xn_ready, m + 1)
                if not isinstance(m, int) or m > 0:
                    pe.wait_ge(row_ready, m)
                for t in range(T):
                    mm = nc.tensor.transpose(tp[:, t * P:(t + 1) * P], xn[:, t, :], ident[:, :])
                mm.then_inc(tr_done, 1)

            def project(m, l):
                pe.wait_ge(hT_ready, m + 1)
                if not isinstance(m, int) or m > 0:
                    pe.wait_ge(wh_ready, 2 * m)
                for t, (k, s) in enumerate(bank_of):
                    nc.tensor.matmul(prj[:, k, s * E:(s + 1) * E], hT[:, t * P:(t + 1) * P],
                                     w_ext[:, l, :], start=(s == 0), stop=True,
                                     skip_group_check=True)
                nc.tensor.matmul(USUM, hsum[:, 0:1].to_broadcast([P, P]), w_ext[:, l, 0:D],
                                 start=False, stop=True, skip_group_check=True).then_inc(prj_done, 1)

            def spread_emax(m):
                pe.wait_ge(emax_ready, m + 1)
                nc.tensor.transpose(tp[:, 0:P], emax[:, 0:1].to_broadcast([P, P]),
                                    ident[:, :]).then_inc(emax_spread, 1)

            def spread_r(m, g):
                pe.wait_ge(vqr_ready, m + 1)
                for t in range(T):
                    mm = nc.tensor.transpose(tp[:, t * P:(t + 1) * P],
                                             vqr[:, g, 2, t:t + 1].to_broadcast([P, P]), ident[:, :])
                mm.then_inc(r_spread, 1)

            def attend(n, g, t):
                if t == 0:
                    pe.wait_ge(wh_ready, 2 * n + 2)
                pe.wait_ge(p_ready, 8 * n + t + 1)
                for i, (k, s) in enumerate(bank_of):
                    if t == 0 and s == 0 and not (isinstance(n, int) and n == 0):
                        pe.wait_ge(acc_copied, NB * (n - 1) + k + 1)
                    mm = nc.tensor.matmul(acc[:, k, s * C:(s + 1) * C],
                                          pbuf[:, t % BUFS, i * P:(i + 1) * P], wh[:, g, t, :],
                                          start=(t == 0 and s == 0), stop=(t == T - 1),
                                          skip_group_check=True)
                    if t == T - 1 and s == NB - 1:
                        mm.then_inc(acc_done, 1)
                mm.then_inc(p_used, 1)

            def setup():
                pe.wait_ge(w_in, 96)
                pe.wait_ge(const_set, 6)
                for l in range(2):
                    mm = nc.tensor.matmul(prj[:, 0, 2 * l:2 * l + 2], w_tr[:, l, :], a_cols[:, l, :],
                                          start=(l == 0), stop=True, skip_group_check=True)
                mm.then_inc(wa_done, 1)
                transposes(0)
                pe.wait_ge(wext_ready, 1)
                project(0, 0)
                spread_emax(0)
                spread_r(0, 0)

            def stage(n, g, l, b, epi, prep, norm_now, norm_next):
                late = 6 if norm_now else 0
                for t in range(T):
                    attend(n, g, t)
                    if prep is not None:
                        if t == 0 + late:
                            transposes(n + 1)
                        if t == 1 + late:
                            project(n + 1, prep)
                        if t == min(2 + late, T - 1):
                            spread_emax(n + 1)
                        if t == min(3 + late, T - 1):
                            spread_r(n + 1, 1 - g)

            schedule(pe, stage, setup, lambda: None)


def kernel(x, adj, L0_gnn_W, L0_gnn_a, L1_gnn_W, L1_gnn_a):
    import numpy as np
    import concourse.bacc as bacc
    from concourse.bass_utils import run_bass_kernel_spmd

    x = np.ascontiguousarray(x)
    b, n, d = x.shape
    t = n // P
    adj = np.asarray(adj).reshape(b, P, t, P, t).transpose(0, 4, 3, 2, 1).reshape(b, t, P, n)
    w0, w1 = np.asarray(L0_gnn_W), np.asarray(L1_gnn_W)
    ins = {
        "x": x, "adj": adj,
        "w0": w0, "w0t": w0.T, "a0": np.asarray(L0_gnn_a).reshape(2, d).T,
        "w1": w1.T, "w1t": w1, "a1": np.asarray(L1_gnn_a).reshape(2, d).T,
    }
    nc = bacc.Bacc("TRN2", target_bir_lowering=False, num_devices=1)
    arrays, aps = {}, []
    for name, a in ins.items():
        a = np.ascontiguousarray(a)
        arrays[f"in_{name}"] = a
        aps.append(nc.dram_tensor(f"in_{name}", a.shape, mybir.dt.from_np(a.dtype),
                                  kind="ExternalInput").ap())
    res = nc.dram_tensor("out_x", x.shape, F32, kind="ExternalOutput").ap()
    gat_two_layers(nc, *aps, res)
    r = run_bass_kernel_spmd(nc, [arrays], core_ids=[0])
    return r.results[0]["out_x"]
```

```python
from contextlib import ExitStack

import concourse.bass as bass
from concourse import mybir

P = 128
F32 = mybir.dt.float32
I32 = mybir.dt.int32
ALU = mybir.AluOpType
ACT = mybir.ActivationFunctionType
AX_X = mybir.AxisListType.X

SLOPE = 0.2
EPS = 1e-5
EMPTY = 2.0 ** -112
Q_SCALE = 2.0 ** 80


def gat_two_layers(nc, x, adj, w0, w0t, a0, w1, w1t, a1, out):
    B, T, _, N = adj.shape
    D = x.shape[2]
    C = D + 1
    E = D + 2
    BANK = 512
    NB = 3
    LAST = 2 * B - 1
    SLOTS = 3
    TAKE_AFTER = 4
    bank_of = [(i // NB, i % NB) for i in range(T)]
    tiles_in = [NB, NB, T - 2 * NB]

    xv = x.rearrange("b (p t) d -> b p (t d)", t=T)
    ov = out.rearrange("b (p t) d -> b p (t d)", t=T)

    with ExitStack() as ctx:
        def sb(name, shape, dt=F32):
            return ctx.enter_context(nc.sbuf_tensor(name, shape, dt))

        def ps(name, shape):
            return ctx.enter_context(nc.psum_tensor(name, shape, F32))

        def sem(name):
            return ctx.enter_context(nc.semaphore(name))

        ident = sb("ident", [P, P])
        neg_half = sb("neg_half", [P, T])
        neg_one = sb("neg_one", [P, 1])
        gate = sb("gate", [P, 1])
        act_gate = sb("act_gate", [P, 1])
        w_ext = sb("w_ext", [P, 2, E])
        w_tr = sb("w_tr", [P, 2, D])
        a_cols = sb("a_cols", [P, 2, 2])
        adj_sb = sb("adj_sb", [P, SLOTS * T * N], I32)
        x0 = sb("x0", [P, SLOTS * T * D])
        x1 = sb("x1", [P, SLOTS * T * D])
        stats = sb("stats", [P, T, 6])
        mean2 = sb("mean2", [P, T])
        mdiff = sb("mdiff", [P, T])
        m2sum = sb("m2sum", [P, T])
        negmean = sb("negmean", [P, T])
        shift = sb("shift", [P, T])
        between = sb("between", [P, T])
        vareps = sb("vareps", [P, T])
        rstd = sb("rstd", [P, T])
        xn = sb("xn", [P, T, D])
        hT = sb("hT", [P, T * P])
        hsum = sb("hsum", [P, 1])
        wh = sb("wh", [P, 2, T, C])
        ecol = sb("ecol", [P, T, 2])
        emax = sb("emax", [P, 1])
        cmax = sb("cmax", [P, 1])
        zrow = sb("zrow", [P, T])
        args = sb("args", [P, 3, T])
        sqr = sb("sqr", [P, 2, 3, T])
        row_r = sb("row_r", [P, 2, N])
        uniform = sb("uniform", [P, 2, C])
        pbuf = sb("pbuf", [P, T, N])
        accs = sb("accs", [P, T, C])
        rec = sb("rec", [P, T])
        hp = sb("hp", [P, T, D])
        ex = sb("ex", [P, T * D])

        acc = ps("acc", [P, NB, BANK])
        prj = ps("prj", [P, NB, BANK])
        tp = ps("tp", [P, 2 * BANK])
        USUM = prj[:, NB - 1, tiles_in[-1] * E:tiles_in[-1] * E + D]

        w_in = sem("w_in")
        x_first = [sem(f"x_first{b}") for b in range(SLOTS)]
        x_in = sem("x_in")
        adj_in = [sem(f"adj_in{t}") for t in range(T)]
        const_set = sem("const_set")
        wa_done = sem("wa_done")
        wext_ready = sem("wext_ready")
        bn_done = sem("bn_done")
        halves_done = sem("halves_done")
        mean_ready = sem("mean_ready")
        vareps_ready = sem("vareps_ready")
        rstd_ready = sem("rstd_ready")
        shift_ready = sem("shift_ready")
        xn_ready = sem("xn_ready")
        tr_done = sem("tr_done")
        hT_ready = sem("hT_ready")
        prj_done = sem("prj_done")
        e_copied = sem("e_copied")
        wh_ready = sem("wh_ready")
        emax_ready = sem("emax_ready")
        emax_spread = sem("emax_spread")
        cmax_ready = sem("cmax_ready")
        z_ready = sem("z_ready")
        args_ready = sem("args_ready")
        sqr_ready = sem("sqr_ready")
        q_ready = sem("q_ready")
        r_spread = sem("r_spread")
        row_ready = sem("row_ready")
        p_ready = sem("p_ready")
        p_used = sem("p_used")
        acc_done = sem("acc_done")
        acc_copied = sem("acc_copied")
        rec_ready = sem("rec_ready")
        hp_ready = sem("hp_ready")
        x0m_ready = sem("x0m_ready")
        ex_ready = sem("ex_ready")
        elu_ready = sem("elu_ready")
        x1_ready = sem("x1_ready")
        out_ready = sem("out_ready")
        out_stored = sem("out_stored")

        def wait_x(eng, b):
            if isinstance(b, int) and b < SLOTS:
                eng.wait_ge(x_first[b], 16)
            else:
                eng.wait_ge(x_in, 16 * (b - SLOTS + 1))

        def x_at(buf, b):
            return buf[:, bass.ds((b % SLOTS) * (T * D), T * D)]

        def x3_at(buf, b):
            return x_at(buf, b).rearrange("p (t d) -> p t d", t=T)

        def adj_at(b, t):
            return adj_sb[:, bass.ds((b % SLOTS) * (T * N) + t * N, N)]

        def schedule(eng, stage, setup, last):
            def pair(b):
                stage(2 * b + 3, 1, 1, b, (0, b + 2), 0, (1, b + 1))
                stage(2 * b + 4, 0, 0, b + 3, (1, b), 1, (0, b + 4))

            setup()
            stage(0, 0, 0, 0, None, 0, (0, 2))
            stage(1, 1, 0, 1, (0, 0), 0, (1, 0))
            stage(2, 0, 0, 2, (0, 1), 1, (0, 3))
            pair(0)
            with eng.Fori(1, B - 4) as b:
                pair(b)
            stage(LAST - 4, 1, 1, B - 4, (0, B - 2), 0, (1, B - 3))
            stage(LAST - 3, 0, 0, B - 1, (1, B - 4), 1, (1, B - 2))
            stage(LAST - 2, 1, 1, B - 3, (0, B - 1), 1, (1, B - 1))
            stage(LAST - 1, 0, 1, B - 2, (1, B - 3), 1, None)
            stage(LAST, 1, 1, B - 1, (1, B - 2), None, None)
            last()

        block = ctx.enter_context(nc.Block())

        @block.sync
        def _(sp):
            def load_adj(b, t):
                sp.dma_start(adj_at(b, t), adj[b, t]).then_inc(adj_in[t], 16)

            def later_x(b):
                sp.wait_ge(x1_ready, b - SLOTS + 1)
                if not isinstance(b, int) or b > SLOTS:
                    sp.wait_ge(x_in, 16 * (b - SLOTS))
                sp.dma_start(x_at(x0, b), xv[b]).then_inc(x_in, 16)

            def later_adj(b):
                for t in range(T):
                    sp.wait_ge(p_ready, T * (2 * b + 3) + t + 1)
                    load_adj(b + SLOTS, t)

            def store(b):
                sp.wait_ge(out_ready, b + 1)
                sp.dma_start(ov[b], x_at(x1, b)).then_inc(out_stored, 16)

            for b in range(2):
                sp.dma_start(x_at(x0, b), xv[b]).then_inc(x_first[b], 16)
            for l, (w, wt, a) in enumerate(((w0, w0t, a0), (w1, w1t, a1))):
                sp.dma_start(w_tr[:, l, :], wt).then_inc(w_in, 16)
                sp.dma_start(a_cols[:, l, :], a).then_inc(w_in, 16)
                sp.dma_start(w_ext[:, l, 0:D], w).then_inc(w_in, 16)
            for t in range(T):
                load_adj(0, t)
            sp.dma_start(x_at(x0, 2), xv[2]).then_inc(x_first[2], 16)
            for b in range(1, SLOTS):
                for t in range(T):
                    sp.wait_ge(adj_in[t], 16 * b)
                    load_adj(b, t)
            later_x(3)
            later_x(4)
            with sp.Fori(0, B - 5) as b:
                later_adj(b)
                later_x(b + 5)
                store(b)
            for b in range(B - 5, B - SLOTS):
                later_adj(b)
                store(b)
            for b in range(B - SLOTS, B):
                store(b)
            sp.wait_ge(out_stored, 16 * B)

        @block.gpsimd
        def _(pool):
            def normaliser(m):
                pool.wait_ge(vareps_ready, m + 1)
                if not isinstance(m, int) or m > 0:
                    pool.wait_ge(xn_ready, T * m)
                nc.gpsimd.tensor_tensor(rstd[:, :], vareps[:, :], neg_half[:, :],
                                        ALU.pow).then_inc(rstd_ready, 1)
                pool.wait_ge(rstd_ready, m + 1)
                nc.gpsimd.tensor_tensor(shift[:, :], negmean[:, :], rstd[:, :],
                                        ALU.mult).then_inc(shift_ready, 1)

            def epilogue(e, l, b):
                if l == 0:
                    wait_x(pool, b)
                    nc.gpsimd.tensor_tensor(x_at(x0, b), x_at(x0, b),
                                            neg_one[:, 0:1].to_broadcast([P, T * D]),
                                            ALU.add).then_inc(x0m_ready, 1)
                if l == 1 and not (isinstance(b, int) and b > B - SLOTS):
                    pool.wait_ge(x1_ready, b + SLOTS)
                elif l == 1:
                    pool.wait_ge(out_ready, b)
                elif not isinstance(b, int) or b >= SLOTS:
                    pool.wait_ge(out_ready, b - 2)
                elif b > 0:
                    pool.wait_ge(x1_ready, b)
                pool.wait_ge(rec_ready, e + 1)
                nc.gpsimd.tensor_tensor(hp[:, :, :], accs[:, :, 0:D],
                                        rec[:, :].unsqueeze(2).to_broadcast([P, T, D]),
                                        ALU.mult).then_inc(hp_ready, 1)
                if l == 1:
                    pool.wait_ge(hp_ready, e + 1)
                    nc.gpsimd.tensor_tensor(x_at(x1, b),
                                            hp[:, :, :].rearrange("p t d -> p (t d)"),
                                            x_at(x1, b), ALU.add).then_inc(out_ready, 1)

            def setup():
                nc.gpsimd.memset(ident[:, :], 0.0).then_inc(const_set, 1)
                pool.wait_ge(const_set, 1)
                nc.gpsimd.affine_select(out=ident[:, :], in_=ident[:, :],
                                        compare_op=ALU.not_equal, fill=1.0, base=0,
                                        pattern=[[-1, P]], channel_multiplier=1).then_inc(const_set, 1)
                nc.gpsimd.memset(neg_half[:, :], -0.5).then_inc(const_set, 1)
                nc.gpsimd.memset(neg_one[:, :], -1.0).then_inc(const_set, 1)
                nc.gpsimd.memset(uniform[:, :, D:C], EMPTY * N).then_inc(const_set, 1)
                pool.wait_ge(const_set, 5)
                normaliser(0)
                normaliser(1)

            def stage(n, g, l, b, epi, prep, norm):
                if epi is not None:
                    epilogue(n - 1, *epi)
                if norm is not None:
                    normaliser(n + 2)

            def last():
                epilogue(LAST, 1, B - 1)

            schedule(pool, stage, setup, last)

        @block.scalar
        def _(act):
            def normalise(m, l, b):
                if not isinstance(m, int) or m > 0:
                    act.wait_ge(tr_done, m)
                act.wait_ge(shift_ready, m + 1)
                nc.scalar.activation(act_gate[:, :], shift[:, 0:1], ACT.Copy)
                src = x3_at(x1 if l else x0, b)
                for t in range(T):
                    nc.scalar.activation(xn[:, t, :], src[:, t, :], ACT.Relu,
                                         bias=shift[:, t:t + 1],
                                         scale=rstd[:, t:t + 1]).then_inc(xn_ready, 1)

            def copy_hT(m):
                act.wait_ge(tr_done, m + 1)
                nc.scalar.activation(hT[:, :], tp[:, :], ACT.Copy,
                                     accum_out=hsum[:, :]).then_inc(hT_ready, 1)

            def exps(m, g):
                act.wait_ge(args_ready, m + 1)
                nc.scalar.activation(sqr[:, g, :, :], args[:, :, :], ACT.Exp).then_inc(sqr_ready, 1)
                act.wait_ge(sqr_ready, m + 1)
                nc.scalar.mul(wh[:, g, :, D], sqr[:, g, 1, :], Q_SCALE).then_inc(q_ready, 1)

            def scale_wh(m, g, tiles):
                act.wait_ge(q_ready, m + 1)
                for t in tiles:
                    k, s = bank_of[t]
                    nc.scalar.activation(wh[:, g, t, 0:D], prj[:, k, s * E:s * E + D], ACT.Copy,
                                         scale=wh[:, g, t, D:C]).then_inc(wh_ready, 1)

            def copy_row(m, g):
                act.wait_ge(r_spread, m + 1)
                nc.scalar.activation(row_r[:, g, :], tp[:, :], ACT.Copy).then_inc(row_ready, 1)

            def elu_exp(e, b):
                act.wait_ge(hp_ready, e + 1)
                if not isinstance(b, int) or b > 0:
                    act.wait_ge(elu_ready, b)
                nc.scalar.activation(ex[:, :], hp[:, :, :].rearrange("p t d -> p (t d)"),
                                     ACT.Exp).then_inc(ex_ready, 1)

            def rows(m, g):
                exps(m, g)
                scale_wh(m, g, range(4))
                copy_row(m, g)
                scale_wh(m, g, range(4, T))

            def setup():
                normalise(0, 0, 0)
                copy_hT(0)
                normalise(1, 0, 1)
                rows(0, 0)
                copy_hT(1)

            def stage(n, g, l, b, epi, prep, norm):
                if epi is not None and epi[0] == 0:
                    elu_exp(n - 1, epi[1])
                if prep is not None:
                    rows(n + 1, 1 - g)
                if norm is not None:
                    normalise(n + 2, *norm)
                    copy_hT(n + 2)

            schedule(act, stage, setup, lambda: None)

        @block.vector
        def _(dve):
            def statistics(m, l, b):
                if l:
                    dve.wait_ge(x1_ready, b + 1)
                else:
                    wait_x(dve, b)
                nc.vector.memset(gate[:, :], 0.0)
                src = x3_at(x1 if l else x0, b)
                for t in range(T):
                    st = nc.vector.bn_stats(stats[:, t, :], src[:, t, :])
                st.then_inc(bn_done, 1)

            def moments(m):
                dve.wait_ge(bn_done, m + 1)
                if not isinstance(m, int) or m > 0:
                    dve.wait_ge(shift_ready, m)
                nc.vector.tensor_tensor(mdiff[:, :], stats[:, :, 1], stats[:, :, 4],
                                        ALU.subtract).then_inc(halves_done, 1)
                nc.vector.scalar_tensor_tensor(m2sum[:, :], stats[:, :, 2], D * EPS, stats[:, :, 5],
                                               ALU.add, ALU.add).then_inc(halves_done, 1)
                nc.vector.tensor_tensor(mean2[:, :], stats[:, :, 1], stats[:, :, 4],
                                        ALU.add).then_inc(halves_done, 1)
                dve.wait_ge(halves_done, 3 * m + 3)
                nc.vector.scalar_tensor_tensor(between[:, :], mdiff[:, :], 0.25, mdiff[:, :],
                                               ALU.mult, ALU.mult).then_inc(mean_ready, 1)
                nc.vector.tensor_scalar(negmean[:, :], mean2[:, :], -0.5, None,
                                        ALU.mult).then_inc(mean_ready, 1)
                dve.wait_ge(mean_ready, 2 * m + 2)
                nc.vector.scalar_tensor_tensor(vareps[:, :], m2sum[:, :], 1.0 / D, between[:, :],
                                               ALU.mult, ALU.add).then_inc(vareps_ready, 1)

            def copy_e(m, g):
                dve.wait_ge(prj_done, m + 1)
                full = prj[:, 0:2, 0:NB * E].rearrange("p b (s e) -> p b s e", e=E)[:, :, :, D:E]
                nc.vector.tensor_copy(ecol[:, 0:2 * NB, :].rearrange("p (b s) e -> p b s e", b=2),
                                      full).then_inc(e_copied, 1)
                part = prj[:, 2, 0:tiles_in[2] * E].rearrange("p (s e) -> p s e", e=E)[:, :, D:E]
                nc.vector.tensor_copy(ecol[:, 2 * NB:T, :], part).then_inc(e_copied, 1)
                nc.vector.tensor_scalar(uniform[:, g, 0:D], USUM, EMPTY, None,
                                        ALU.mult).then_inc(e_copied, 1)
                dve.wait_ge(e_copied, 3 * m + 3)
                nc.vector.tensor_reduce(emax[:, :], ecol[:, :, 1], AX_X, ALU.max).then_inc(emax_ready, 1)

            def exp_args(m):
                dve.wait_ge(emax_spread, m + 1)
                nc.vector.tensor_reduce(cmax[:, :], tp[:, 0:P], AX_X, ALU.max).then_inc(cmax_ready, 1)
                dve.wait_ge(cmax_ready, m + 1)
                nc.vector.tensor_scalar(zrow[:, :], ecol[:, :, 0], cmax[:, 0:1], 0.0, ALU.add,
                                        ALU.max).then_inc(z_ready, 1)
                nc.vector.tensor_scalar(args[:, 0, :], ecol[:, :, 1], cmax[:, 0:1], 1.0 - SLOPE,
                                        ALU.subtract, ALU.mult)
                nc.vector.tensor_scalar(args[:, 1, :], ecol[:, :, 1], cmax[:, 0:1], SLOPE,
                                        ALU.subtract, ALU.mult)
                dve.wait_ge(z_ready, m + 1)
                nc.vector.tensor_scalar(args[:, 2, :], zrow[:, :], SLOPE - 1.0, None,
                                        ALU.mult).then_inc(args_ready, 1)

            def mask(n, g, l, b, t):
                if l == 0:
                    dve.wait_ge(adj_in[t], 16 * (b + 1))
                if (not isinstance(n, int) or n > 0) and t in (0, 3):
                    dve.wait_ge(p_used, T * (n - 1) + (3 if t == 0 else TAKE_AFTER + 1))
                if t == 0:
                    dve.wait_ge(row_ready, n + 1)
                nc.vector.scalar_tensor_tensor(
                    pbuf[:, t, :], row_r[:, g, :], sqr[:, g, 0, t:t + 1],
                    adj_at(b, t),
                    ALU.max, ALU.min).then_inc(p_ready, 1)

            def copy_acc(e, g, k):
                if k == 0 and not (isinstance(e, int) and e == 0):
                    dve.wait_ge(hp_ready, e)
                if k < 2:
                    dve.wait_ge(acc_done, 2 * e + k + 1)
                else:
                    dve.wait_ge(p_used, 8 * e + 8)
                w = tiles_in[k]
                nc.vector.tensor_tensor(
                    accs[:, k * NB:k * NB + w, :],
                    acc[:, k, 0:w * C].rearrange("p (s c) -> p s c", c=C),
                    uniform[:, g, :].unsqueeze(1).to_broadcast([P, w, C]),
                    ALU.add).then_inc(acc_copied, 1)

            def take_acc(e, g):
                for k in range(NB):
                    copy_acc(e, g, k)
                dve.wait_ge(acc_copied, NB * e + NB)
                nc.vector.reciprocal(rec[:, :], accs[:, :, D]).then_inc(rec_ready, 1)

            def elu_half(b):
                dve.wait_ge(ex_ready, b + 1)
                dve.wait_ge(x0m_ready, b + 1)
                nc.vector.scalar_tensor_tensor(ex[:, :], ex[:, :], 1.0, x_at(x0, b), ALU.min,
                                               ALU.add).then_inc(elu_ready, 1)

            def elu_rest(b):
                dve.wait_ge(elu_ready, b + 1)
                if not isinstance(b, int) or b >= SLOTS:
                    dve.wait_ge(out_stored, 16 * (b - SLOTS + 1))
                nc.vector.scalar_tensor_tensor(
                    x_at(x1, b), hp[:, :, :].rearrange("p t d -> p (t d)"), 0.0, ex[:, :],
                    ALU.max, ALU.add).then_inc(x1_ready, 1)

            def elu_residual(b):
                elu_half(b)
                elu_rest(b)

            def setup():
                statistics(0, 0, 0)
                moments(0)
                dve.wait_ge(wa_done, 1)
                nc.vector.tensor_copy(w_ext[:, :, D:E],
                                      prj[:, 0, 0:4].rearrange("p (l e) -> p l e", l=2)
                                      ).then_inc(wext_ready, 1)
                statistics(1, 0, 1)
                moments(1)
                copy_e(0, 0)
                exp_args(0)

            def stage(n, g, l, b, epi, prep, norm):
                def masks(*tiles):
                    for t in tiles:
                        mask(n, g, l, b, t)

                masks(*range(TAKE_AFTER + 1))
                if epi is not None:
                    take_acc(n - 1, 1 - g)
                masks(5)
                if prep is not None:
                    copy_e(n + 1, 1 - g)
                masks(6)
                if prep is not None:
                    exp_args(n + 1)
                if epi is not None and epi[0] == 0:
                    elu_residual(epi[1])
                if norm is not None:
                    statistics(n + 2, *norm)
                    moments(n + 2)
                masks(7)

            schedule(dve, stage, setup, lambda: take_acc(LAST, 1))

        @block.tensor
        def _(pe):
            def transposes(m):
                pe.wait_ge(xn_ready, T * m + T)
                if not isinstance(m, int) or m > 0:
                    pe.wait_ge(row_ready, m)
                for t in range(T):
                    mm = nc.tensor.transpose(tp[:, t * P:(t + 1) * P], xn[:, t, :], ident[:, :])
                mm.then_inc(tr_done, 1)

            def project(m, l):
                pe.wait_ge(hT_ready, m + 1)
                if not isinstance(m, int) or m > 0:
                    pe.wait_ge(wh_ready, T * m)
                for t, (k, s) in enumerate(bank_of):
                    nc.tensor.matmul(prj[:, k, s * E:(s + 1) * E], hT[:, t * P:(t + 1) * P],
                                     w_ext[:, l, :], start=(s == 0), stop=True,
                                     skip_group_check=True)
                nc.tensor.matmul(USUM, hsum[:, 0:1].to_broadcast([P, P]), w_ext[:, l, 0:D],
                                 start=False, stop=True, skip_group_check=True).then_inc(prj_done, 1)

            def spread_emax(m):
                pe.wait_ge(emax_ready, m + 1)
                nc.tensor.transpose(tp[:, 0:P], emax[:, 0:1].to_broadcast([P, P]),
                                    ident[:, :]).then_inc(emax_spread, 1)

            def spread_r(m, g):
                pe.wait_ge(sqr_ready, m + 1)
                for t in range(T):
                    mm = nc.tensor.transpose(tp[:, t * P:(t + 1) * P],
                                             sqr[:, g, 2, t:t + 1].to_broadcast([P, P]), ident[:, :])
                mm.then_inc(r_spread, 1)

            def attend(n, g, t):
                if t % 4 == 0:
                    pe.wait_ge(wh_ready, T * n + t + 4)
                pe.wait_ge(p_ready, T * n + t + 1)
                for i, (k, s) in enumerate(bank_of):
                    if t == 0 and s == 0 and not (isinstance(n, int) and n == 0):
                        pe.wait_ge(acc_copied, NB * (n - 1) + k + 1)
                    mm = nc.tensor.matmul(acc[:, k, s * C:(s + 1) * C],
                                          pbuf[:, t, i * P:(i + 1) * P], wh[:, g, t, :],
                                          start=(t == 0 and s == 0), stop=(t == T - 1),
                                          skip_group_check=True)
                    if t == T - 1 and s == NB - 1:
                        mm.then_inc(acc_done, 1)
                mm.then_inc(p_used, 1)

            def setup():
                pe.wait_ge(w_in, 96)
                pe.wait_ge(const_set, 5)
                for l in range(2):
                    mm = nc.tensor.matmul(prj[:, 0, 2 * l:2 * l + 2], w_tr[:, l, :], a_cols[:, l, :],
                                          start=(l == 0), stop=True, skip_group_check=True)
                mm.then_inc(wa_done, 1)
                transposes(0)
                pe.wait_ge(wext_ready, 1)
                project(0, 0)
                spread_emax(0)
                spread_r(0, 0)
                transposes(1)

            def stage(n, g, l, b, epi, prep, norm):
                if prep is not None:
                    project(n + 1, prep)
                attend(n, g, 0)
                if prep is not None:
                    spread_emax(n + 1)
                attend(n, g, 1)
                if prep is not None:
                    spread_r(n + 1, 1 - g)
                for t in range(2, T - 1):
                    attend(n, g, t)
                if norm is not None:
                    transposes(n + 2)
                attend(n, g, T - 1)

            schedule(pe, stage, setup, lambda: None)


def kernel(x, adj, L0_gnn_W, L0_gnn_a, L1_gnn_W, L1_gnn_a):
    import numpy as np
    import concourse.bacc as bacc
    from concourse.bass_utils import run_bass_kernel_spmd

    x = np.ascontiguousarray(x)
    b, n, d = x.shape
    t = n // P
    adj = np.asarray(adj).reshape(b, P, t, P, t).transpose(0, 4, 3, 2, 1).reshape(b, t, P, n)
    w0, w1 = np.asarray(L0_gnn_W), np.asarray(L1_gnn_W)
    ins = {
        "x": x, "adj": adj,
        "w0": w0, "w0t": w0.T, "a0": np.asarray(L0_gnn_a).reshape(2, d).T,
        "w1": w1.T, "w1t": w1, "a1": np.asarray(L1_gnn_a).reshape(2, d).T,
    }
    nc = bacc.Bacc("TRN2", target_bir_lowering=False, num_devices=1)
    arrays, aps = {}, []
    for name, a in ins.items():
        a = np.ascontiguousarray(a)
        arrays[f"in_{name}"] = a
        aps.append(nc.dram_tensor(f"in_{name}", a.shape, mybir.dt.from_np(a.dtype),
                                  kind="ExternalInput").ap())
    res = nc.dram_tensor("out_x", x.shape, F32, kind="ExternalOutput").ap()
    gat_two_layers(nc, *aps, res)
    r = run_bass_kernel_spmd(nc, [arrays], core_ids=[0])
    return r.results[0]["out_x"]
```

```python
from contextlib import ExitStack

import concourse.bass as bass
from concourse import mybir

P = 128
F32 = mybir.dt.float32
I32 = mybir.dt.int32
ALU = mybir.AluOpType
ACT = mybir.ActivationFunctionType
AX_X = mybir.AxisListType.X

SLOPE = 0.2
EPS = 1e-5
EMPTY = 2.0 ** -112
Q_SCALE = 2.0 ** 80


def gat_two_layers(nc, x, adj, w0, w0t, a0, w1, w1t, a1, r_rows, out):
    B, T, _, N = adj.shape
    D = x.shape[2]
    C = D + 1
    E = D + 2
    BANK = 512
    NB = 3
    LAST = 2 * B - 1
    SLOTS = 3
    TAKE_AFTER = 3
    LAST_SPLIT = T // 2
    DVE_SHARE = 5
    WARM = (24, 10, 8, 8, 10)
    NORM_LATE = (1, LAST - 2)
    bank_of = [(i // NB, i % NB) for i in range(T)]
    tiles_in = [NB, NB, T - 2 * NB]

    xv = x.rearrange("b (p t) d -> b p (t d)", t=T)
    ov = out.rearrange("b (p t) d -> b p (t d)", t=T)

    with ExitStack() as ctx:
        def sb(name, shape, dt=F32):
            return ctx.enter_context(nc.sbuf_tensor(name, shape, dt))

        def ps(name, shape):
            return ctx.enter_context(nc.psum_tensor(name, shape, F32))

        def sem(name):
            return ctx.enter_context(nc.semaphore(name))

        ident = sb("ident", [P, P])
        neg_half = sb("neg_half", [P, T])
        neg_one = sb("neg_one", [P, 1])
        gate = sb("gate", [P, 1])
        rT = sb("rT", [T, P])
        act_gate = sb("act_gate", [P, 1])
        w_ext = sb("w_ext", [P, 2, E])
        w_tr = sb("w_tr", [P, 2, D])
        a_cols = sb("a_cols", [P, 2, 2])
        adj_sb = sb("adj_sb", [P, SLOTS * T * N], I32)
        x0 = sb("x0", [P, SLOTS * T * D])
        x1 = sb("x1", [P, SLOTS * T * D])
        stats = sb("stats", [P, T, 6])
        mean2 = sb("mean2", [P, T])
        mdiff = sb("mdiff", [P, T])
        m2sum = sb("m2sum", [P, T])
        negmean = sb("negmean", [P, T])
        shift = sb("shift", [P, T])
        between = sb("between", [P, T])
        vareps = sb("vareps", [P, T])
        rstd = sb("rstd", [P, T])
        xn = sb("xn", [P, T, D])
        hT = sb("hT", [P, T * P])
        hsum = sb("hsum", [P, 1])
        wh = sb("wh", [P, 2, T, C])
        ecol = sb("ecol", [P, T, 2])
        emax = sb("emax", [P, 1])
        cmax = sb("cmax", [P, 1])
        zrow = sb("zrow", [P, T])
        args = sb("args", [P, 3, T])
        sqr = sb("sqr", [P, 2, 3, T])
        row_r = sb("row_r", [P, 2, N])
        uniform = sb("uniform", [P, 2, C])
        pbuf = sb("pbuf", [P, T, N])
        accs = sb("accs", [P, T, C])
        rec = sb("rec", [P, T])
        hp = sb("hp", [P, T, D])
        ex = sb("ex", [P, T * D])

        acc = ps("acc", [P, NB, BANK])
        prj = ps("prj", [P, NB, BANK])
        tp = ps("tp", [P, 2 * BANK])
        USUM = prj[:, NB - 1, tiles_in[-1] * E:tiles_in[-1] * E + D]

        w_in = sem("w_in")
        x_half = sem("x_half")
        xn_dve = sem("xn_dve")
        row0_dve = sem("row0_dve")
        p_half = sem("p_half")
        x_first = [sem(f"x_first{b}") for b in range(SLOTS)]
        x_in = sem("x_in")
        adj_in = [sem(f"adj_in{t}") for t in range(T)]
        const_set = sem("const_set")
        wa_done = sem("wa_done")
        wext_ready = sem("wext_ready")
        bn_done = sem("bn_done")
        halves_done = sem("halves_done")
        mean_ready = sem("mean_ready")
        vareps_ready = sem("vareps_ready")
        rstd_ready = sem("rstd_ready")
        shift_ready = sem("shift_ready")
        xn_ready = sem("xn_ready")
        tr_done = sem("tr_done")
        hT_ready = sem("hT_ready")
        prj_done = sem("prj_done")
        e_copied = sem("e_copied")
        wh_ready = sem("wh_ready")
        emax_ready = sem("emax_ready")
        emax_spread = sem("emax_spread")
        cmax_ready = sem("cmax_ready")
        z_ready = sem("z_ready")
        args_ready = sem("args_ready")
        sqr_ready = sem("sqr_ready")
        q_ready = sem("q_ready")
        r_spread = sem("r_spread")
        row0_ready = sem("row0_ready")
        r_turned = sem("r_turned")
        rT_ready = sem("rT_ready")
        r_written = sem("r_written")
        row_in = sem("row_in")
        p_ready = sem("p_ready")
        p_used = sem("p_used")
        acc_done = sem("acc_done")
        acc_copied = sem("acc_copied")
        rec_ready = sem("rec_ready")
        last_rec = sem("last_rec")
        last_ready = sem("last_ready")
        hp_ready = sem("hp_ready")
        x0m_ready = sem("x0m_ready")
        ex_ready = sem("ex_ready")
        elu_ready = sem("elu_ready")
        x1_ready = sem("x1_ready")
        out_ready = sem("out_ready")
        out_stored = sem("out_stored")

        def wait_x(eng, b):
            if isinstance(b, int) and b < SLOTS:
                if b == 0:
                    eng.wait_ge(x_half, 16)
                eng.wait_ge(x_first[b], 16)
            else:
                eng.wait_ge(x_in, 16 * (b - SLOTS + 1))

        def xn_before(m):
            return T * m - DVE_SHARE

        def x_at(buf, b):
            return buf[:, bass.ds((b % SLOTS) * (T * D), T * D)]

        def x3_at(buf, b):
            return x_at(buf, b).rearrange("p (t d) -> p t d", t=T)

        def adj_at(b, t):
            return adj_sb[:, bass.ds((b % SLOTS) * (T * N) + t * N, N)]

        def schedule(eng, stage, setup, last):
            def pair(b):
                stage(2 * b + 3, 1, 1, b, (0, b + 2), 0, (1, b + 1))
                stage(2 * b + 4, 0, 0, b + 3, (1, b), 1, (0, b + 4))

            setup()
            stage(0, 0, 0, 0, None, 0, (0, 2))
            stage(1, 1, 0, 1, (0, 0), 0, (1, 0))
            stage(2, 0, 0, 2, (0, 1), 1, (0, 3))
            pair(0)
            with eng.Fori(1, B - 4) as b:
                pair(b)
            stage(LAST - 4, 1, 1, B - 4, (0, B - 2), 0, (1, B - 3))
            stage(LAST - 3, 0, 0, B - 1, (1, B - 4), 1, (1, B - 2))
            stage(LAST - 2, 1, 1, B - 3, (0, B - 1), 1, (1, B - 1))
            stage(LAST - 1, 0, 1, B - 2, (1, B - 3), 1, None)
            stage(LAST, 1, 1, B - 1, (1, B - 2), None, None)
            last()

        def first(n):
            return isinstance(n, int) and n == 0

        def norm_is_late(n):
            return isinstance(n, int) and n in NORM_LATE

        block = ctx.enter_context(nc.Block())

        @block.sync
        def _(sp):
            def load_adj(b, t):
                sp.dma_start(adj_at(b, t), adj[b, t]).then_inc(adj_in[t], 16)

            def later_x(b):
                sp.wait_ge(x1_ready, b - SLOTS + 1)
                if not isinstance(b, int) or b > SLOTS:
                    sp.wait_ge(x_in, 16 * (b - SLOTS))
                sp.dma_start(x_at(x0, b), xv[b]).then_inc(x_in, 16)

            def next_adj(b, tiles):
                for t in tiles:
                    sp.wait_ge(adj_in[t], 16 * b)
                    load_adj(b, t)

            def later_adj(b, tiles):
                for t in tiles:
                    sp.wait_ge(p_ready, T * (2 * b + 3) + t + 1)
                    load_adj(b + SLOTS, t)

            def write_r(m):
                sp.wait_ge(rT_ready, m)
                sp.dma_start(r_rows, rT[:, :]).then_inc(r_written, 16)

            def spread_row(m, g):
                sp.wait_ge(r_written, 16 * m)
                sp.dma_start(row_r[:, g, :],
                             r_rows.rearrange("t p -> (t p)").partition_broadcast(P)
                             ).then_inc(row_in, 16)

            def load_row(m, g):
                write_r(m)
                spread_row(m, g)

            def store(b):
                sp.wait_ge(out_ready, b + 1)
                sp.dma_start(ov[b], x_at(x1, b)).then_inc(out_stored, 16)

            half = T * D // 2
            sp.dma_start(x0[:, 0:half], xv[0][:, 0:half]).then_inc(x_half, 16)
            sp.dma_start(x0[:, half:2 * half], xv[0][:, half:2 * half]).then_inc(x_first[0], 16)
            sp.dma_start(x_at(x0, 1), xv[1]).then_inc(x_first[1], 16)
            for l, (w, wt, a) in enumerate(((w0, w0t, a0), (w1, w1t, a1))):
                sp.dma_start(w_tr[:, l, :], wt).then_inc(w_in, 16)
                sp.dma_start(a_cols[:, l, :], a).then_inc(w_in, 16)
                sp.dma_start(w_ext[:, l, 0:D], w).then_inc(w_in, 16)
            sp.dma_start(x_at(x0, 2), xv[2]).then_inc(x_first[2], 16)
            for t in range(T):
                load_adj(0, t)
            next_adj(1, range(4))
            write_r(1)
            next_adj(1, [4])
            spread_row(1, 1)
            next_adj(1, range(5, T))
            next_adj(2, range(5))
            load_row(2, 0)
            next_adj(2, range(5, T))
            later_x(3)
            load_row(3, 1)
            later_x(4)

            def two_stages(b, x_too):
                later_adj(b, range(TAKE_AFTER + 2))
                load_row(2 * b + 4, 0)
                later_adj(b, range(TAKE_AFTER + 2, T))
                if x_too:
                    later_x(b + 5)
                write_r(2 * b + 5)
                store(b)
                spread_row(2 * b + 5, 1)

            with sp.Fori(0, B - 5) as b:
                two_stages(b, True)
            for b in range(B - 5, B - SLOTS):
                two_stages(b, False)
            load_row(LAST - 1, 0)
            store(B - 3)
            load_row(LAST, 1)
            store(B - 2)
            for k in range(NB):
                sp.wait_ge(last_ready, k + 1)
                lo, hi = k * NB * D, (k * NB + tiles_in[k]) * D
                sp.dma_start(ov[B - 1][:, lo:hi],
                             x_at(x1, B - 1)[:, lo:hi]).then_inc(out_stored, 16)
            sp.wait_ge(out_stored, 16 * (B - 1 + NB))

        @block.gpsimd
        def _(pool):
            def normaliser(m):
                pool.wait_ge(vareps_ready, m + 1)
                if not isinstance(m, int) or m > 0:
                    pool.wait_ge(xn_ready, xn_before(m))
                if isinstance(m, int) and m == 1:
                    pool.wait_ge(xn_dve, DVE_SHARE)
                nc.gpsimd.tensor_tensor(rstd[:, :], vareps[:, :], neg_half[:, :],
                                        ALU.pow).then_inc(rstd_ready, 1)
                pool.wait_ge(rstd_ready, m + 1)
                nc.gpsimd.tensor_tensor(shift[:, :], negmean[:, :], rstd[:, :],
                                        ALU.mult).then_inc(shift_ready, 1)

            def epilogue(e, l, b):
                if l == 0:
                    wait_x(pool, b)
                    nc.gpsimd.tensor_tensor(x_at(x0, b), x_at(x0, b),
                                            neg_one[:, 0:1].to_broadcast([P, T * D]),
                                            ALU.add).then_inc(x0m_ready, 1)
                if l == 1 and not (isinstance(b, int) and b > B - SLOTS):
                    pool.wait_ge(x1_ready, b + SLOTS)
                elif l == 1:
                    pool.wait_ge(out_ready, b)
                elif not isinstance(b, int) or b >= SLOTS:
                    pool.wait_ge(out_ready, b - 2)
                elif b > 0:
                    pool.wait_ge(x1_ready, b)
                pool.wait_ge(rec_ready, e + 1)
                nc.gpsimd.tensor_tensor(hp[:, :, :], accs[:, :, 0:D],
                                        rec[:, :].unsqueeze(2).to_broadcast([P, T, D]),
                                        ALU.mult).then_inc(hp_ready, 1)
                if l == 1:
                    pool.wait_ge(hp_ready, e + 1)
                    nc.gpsimd.tensor_tensor(x_at(x1, b),
                                            hp[:, :, :].rearrange("p t d -> p (t d)"),
                                            x_at(x1, b), ALU.add).then_inc(out_ready, 1)

            def setup():
                nc.gpsimd.memset(ident[:, :], 0.0).then_inc(const_set, 1)
                pool.wait_ge(const_set, 1)
                nc.gpsimd.affine_select(out=ident[:, :], in_=ident[:, :],
                                        compare_op=ALU.not_equal, fill=1.0, base=0,
                                        pattern=[[-1, P]], channel_multiplier=1).then_inc(const_set, 1)
                nc.gpsimd.memset(neg_half[:, :], -0.5).then_inc(const_set, 1)
                nc.gpsimd.memset(neg_one[:, :], -1.0).then_inc(const_set, 1)
                nc.gpsimd.memset(uniform[:, :, D:C], EMPTY * N).then_inc(const_set, 1)
                pool.wait_ge(const_set, 5)
                normaliser(0)
                normaliser(1)
                normaliser(2)

            def stage(n, g, l, b, epi, prep, norm):
                if epi is not None:
                    epilogue(n - 1, *epi)
                if norm is not None and not first(n):
                    normaliser(n + 2)

            schedule(pool, stage, setup, lambda: None)

        @block.scalar
        def _(act):
            def normalise(m, l, b):
                if not isinstance(m, int) or m > 0:
                    act.wait_ge(tr_done, m)
                act.wait_ge(shift_ready, m + 1)
                nc.scalar.activation(act_gate[:, :], shift[:, 0:1], ACT.Copy)
                src = x3_at(x1 if l else x0, b)
                for t in range(DVE_SHARE if isinstance(m, int) and m == 0 else 0, T):
                    nc.scalar.activation(xn[:, t, :], src[:, t, :], ACT.Identity,
                                         bias=shift[:, t:t + 1],
                                         scale=rstd[:, t:t + 1]).then_inc(xn_ready, 1)

            def copy_hT(m):
                act.wait_ge(tr_done, m + 1)
                nc.scalar.activation(hT[:, :], tp[:, :], ACT.Relu,
                                     accum_out=hsum[:, :]).then_inc(hT_ready, 1)

            def exps(m, g):
                act.wait_ge(args_ready, m + 1)
                nc.scalar.activation(sqr[:, g, :, :], args[:, :, :], ACT.Exp).then_inc(sqr_ready, 1)
                act.wait_ge(sqr_ready, m + 1)
                nc.scalar.mul(wh[:, g, :, D], sqr[:, g, 1, :], Q_SCALE).then_inc(q_ready, 1)

            def scale_wh(m, g, tiles):
                act.wait_ge(q_ready, m + 1)
                for t in tiles:
                    k, s = bank_of[t]
                    nc.scalar.activation(wh[:, g, t, 0:D], prj[:, k, s * E:s * E + D], ACT.Copy,
                                         scale=wh[:, g, t, D:C]).then_inc(wh_ready, 1)

            def copy_r(m, g):
                if isinstance(m, int) and m == 0:
                    act.wait_ge(r_spread, 1)
                    nc.scalar.activation(row_r[:, g, 0:N // 2], tp[:, 0:N // 2],
                                         ACT.Copy).then_inc(row0_ready, 1)
                else:
                    act.wait_ge(r_turned, m)
                    nc.scalar.activation(rT[:, :], tp[0:T, 0:P], ACT.Copy).then_inc(rT_ready, 1)

            def elu_exp(e, b):
                act.wait_ge(hp_ready, e + 1)
                if not isinstance(b, int) or b > 0:
                    act.wait_ge(elu_ready, b)
                nc.scalar.activation(ex[:, :], hp[:, :, :].rearrange("p t d -> p (t d)"),
                                     ACT.Exp).then_inc(ex_ready, 1)

            def rows(m, g):
                before = 2 if isinstance(m, int) and m == 0 else 4
                exps(m, g)
                scale_wh(m, g, range(before))
                copy_r(m, g)
                scale_wh(m, g, range(before, T))

            def setup():
                normalise(0, 0, 0)
                copy_hT(0)
                normalise(1, 0, 1)
                rows(0, 0)
                copy_hT(1)
                normalise(2, 0, 2)

            def stage(n, g, l, b, epi, prep, norm):
                if epi is not None and epi[0] == 0:
                    elu_exp(n - 1, epi[1])
                if prep is not None:
                    rows(n + 1, 1 - g)
                if norm is not None:
                    if not first(n):
                        normalise(n + 2, *norm)
                    copy_hT(n + 2)

            schedule(act, stage, setup, lambda: None)

        @block.vector
        def _(dve):
            def statistics(m, l, b):
                if l:
                    dve.wait_ge(x1_ready, b + 1)
                elif isinstance(b, int) and b == 0:
                    dve.wait_ge(x_half, 16)
                else:
                    wait_x(dve, b)
                nc.vector.memset(gate[:, :], 0.0)
                src = x3_at(x1 if l else x0, b)
                for t in range(T):
                    if l == 0 and isinstance(b, int) and b == 0 and t == T // 2:
                        dve.wait_ge(x_first[0], 16)
                    st = nc.vector.bn_stats(stats[:, t, :], src[:, t, :])
                st.then_inc(bn_done, 1)

            def moments(m):
                dve.wait_ge(bn_done, m + 1)
                if not isinstance(m, int) or m > 0:
                    dve.wait_ge(shift_ready, m)
                nc.vector.tensor_tensor(mdiff[:, :], stats[:, :, 1], stats[:, :, 4],
                                        ALU.subtract).then_inc(halves_done, 1)
                nc.vector.scalar_tensor_tensor(m2sum[:, :], stats[:, :, 2], D * EPS, stats[:, :, 5],
                                               ALU.add, ALU.add).then_inc(halves_done, 1)
                nc.vector.tensor_tensor(mean2[:, :], stats[:, :, 1], stats[:, :, 4],
                                        ALU.add).then_inc(halves_done, 1)
                dve.wait_ge(halves_done, 3 * m + 3)
                nc.vector.scalar_tensor_tensor(between[:, :], mdiff[:, :], 0.25, mdiff[:, :],
                                               ALU.mult, ALU.mult).then_inc(mean_ready, 1)
                nc.vector.tensor_scalar(negmean[:, :], mean2[:, :], -0.5, None,
                                        ALU.mult).then_inc(mean_ready, 1)
                dve.wait_ge(mean_ready, 2 * m + 2)
                nc.vector.scalar_tensor_tensor(vareps[:, :], m2sum[:, :], 1.0 / D, between[:, :],
                                               ALU.mult, ALU.add).then_inc(vareps_ready, 1)

            def copy_e(m, g):
                dve.wait_ge(prj_done, m + 1)
                full = prj[:, 0:2, 0:NB * E].rearrange("p b (s e) -> p b s e", e=E)[:, :, :, D:E]
                nc.vector.tensor_copy(ecol[:, 0:2 * NB, :].rearrange("p (b s) e -> p b s e", b=2),
                                      full).then_inc(e_copied, 1)
                part = prj[:, 2, 0:tiles_in[2] * E].rearrange("p (s e) -> p s e", e=E)[:, :, D:E]
                nc.vector.tensor_copy(ecol[:, 2 * NB:T, :], part).then_inc(e_copied, 1)
                nc.vector.tensor_scalar(uniform[:, g, 0:D], USUM, EMPTY, None,
                                        ALU.mult).then_inc(e_copied, 1)
                dve.wait_ge(e_copied, 3 * m + 3)
                nc.vector.tensor_reduce(emax[:, :], ecol[:, :, 1], AX_X, ALU.max).then_inc(emax_ready, 1)

            def exp_args(m):
                dve.wait_ge(emax_spread, m + 1)
                nc.vector.tensor_reduce(cmax[:, :], tp[:, 0:P], AX_X, ALU.max).then_inc(cmax_ready, 1)
                dve.wait_ge(cmax_ready, m + 1)
                nc.vector.tensor_scalar(zrow[:, :], ecol[:, :, 0], cmax[:, 0:1], 0.0, ALU.add,
                                        ALU.max).then_inc(z_ready, 1)
                nc.vector.tensor_scalar(args[:, 0, :], ecol[:, :, 1], cmax[:, 0:1], 1.0 - SLOPE,
                                        ALU.subtract, ALU.mult)
                nc.vector.tensor_scalar(args[:, 1, :], ecol[:, :, 1], cmax[:, 0:1], SLOPE,
                                        ALU.subtract, ALU.mult)
                dve.wait_ge(z_ready, m + 1)
                nc.vector.tensor_scalar(args[:, 2, :], zrow[:, :], SLOPE - 1.0, None,
                                        ALU.mult).then_inc(args_ready, 1)

            def mask(n, g, l, b, t):
                if l == 0:
                    dve.wait_ge(adj_in[t], 16 * (b + 1))
                if not first(n) and t == 0:
                    dve.wait_ge(p_used, n)
                if t == 0:
                    dve.wait_ge(row_in, 16 * n)
                nc.vector.scalar_tensor_tensor(pbuf[:, t, :], row_r[:, g, :],
                                               sqr[:, g, 0, t:t + 1], adj_at(b, t),
                                               ALU.max, ALU.min).then_inc(p_ready, 1)

            def mask_part(g, b, t, cols):
                dve.wait_ge(adj_in[t], 16)
                return nc.vector.scalar_tensor_tensor(pbuf[:, t, cols], row_r[:, g, cols],
                                                      sqr[:, g, 0, t:t + 1],
                                                      adj_at(b, t)[:, cols], ALU.max, ALU.min)

            def copy_acc(e, g, k):
                if k == 0 and not (isinstance(e, int) and e == 0):
                    dve.wait_ge(hp_ready, e)
                dve.wait_ge(acc_done, NB * e + k + 1)
                w = tiles_in[k]
                nc.vector.tensor_tensor(
                    accs[:, k * NB:k * NB + w, :],
                    acc[:, k, 0:w * C].rearrange("p (s c) -> p s c", c=C),
                    uniform[:, g, :].unsqueeze(1).to_broadcast([P, w, C]),
                    ALU.add).then_inc(acc_copied, 1)

            def take_acc(e, g):
                for k in range(NB):
                    copy_acc(e, g, k)
                dve.wait_ge(acc_copied, NB * e + NB)
                nc.vector.reciprocal(rec[:, :], accs[:, :, D]).then_inc(rec_ready, 1)

            def elu_half(b):
                dve.wait_ge(x0m_ready, b + 1)
                dve.wait_ge(ex_ready, b + 1)
                nc.vector.scalar_tensor_tensor(ex[:, :], ex[:, :], 1.0, x_at(x0, b), ALU.min,
                                               ALU.add).then_inc(elu_ready, 1)

            def elu_rest(b):
                dve.wait_ge(elu_ready, b + 1)
                if not isinstance(b, int) or b >= SLOTS:
                    dve.wait_ge(out_stored, 16 * (b - SLOTS + 1))
                nc.vector.scalar_tensor_tensor(
                    x_at(x1, b), hp[:, :, :].rearrange("p t d -> p (t d)"), 0.0, ex[:, :],
                    ALU.max, ALU.add).then_inc(x1_ready, 1)

            def setup():
                statistics(0, 0, 0)
                moments(0)
                statistics(1, 0, 1)
                dve.wait_ge(wa_done, 1)
                nc.vector.tensor_copy(w_ext[:, :, D:E],
                                      prj[:, 0, 0:4].rearrange("p (l e) -> p l e", l=2)
                                      ).then_inc(wext_ready, 1)
                dve.wait_ge(shift_ready, 1)
                for t in range(DVE_SHARE):
                    nc.vector.tensor_scalar(xn[:, t, :], x3_at(x0, 0)[:, t, :], rstd[:, t:t + 1],
                                            shift[:, t:t + 1], ALU.mult,
                                            ALU.add).then_inc(xn_dve, 1)
                moments(1)
                statistics(2, 0, 2)
                moments(2)
                copy_e(0, 0)
                exp_args(0)
                dve.wait_ge(r_spread, 2)
                nc.vector.tensor_copy(row_r[:, 0, N // 2:N],
                                      tp[:, N // 2:N]).then_inc(row0_dve, 1)
                dve.wait_ge(row0_ready, 1)
                mask_part(0, 0, 0, slice(0, N // 2)).then_inc(p_half, 1)
                dve.wait_ge(row0_dve, 1)
                mask_part(0, 0, 0, slice(N // 2, N)).then_inc(p_ready, 1)

            def stage(n, g, l, b, epi, prep, norm):
                def masks(*tiles):
                    for t in tiles:
                        mask(n, g, l, b, t)

                def elu(*parts):
                    if epi is not None and epi[0] == 0:
                        for part in parts:
                            part(epi[1])

                def layernorm():
                    if norm is not None:
                        statistics(n + 2, *norm)
                        moments(n + 2)

                def prep_e():
                    if prep is not None:
                        copy_e(n + 1, 1 - g)

                def prep_args():
                    if prep is not None:
                        exp_args(n + 1)

                if first(n):
                    masks(1, 2)
                    prep_e()
                    masks(3)
                    prep_args()
                    masks(4, 5, 6, 7)
                    return
                if isinstance(n, int) and n == LAST:
                    masks(0, 1)
                    take_acc(n - 1, 1 - g)
                    masks(*range(2, T))
                    return
                masks(*range(TAKE_AFTER + 1))
                take_acc(n - 1, 1 - g)
                prep_e()
                masks(4)
                prep_args()
                if norm_is_late(n):
                    elu(elu_half, elu_rest)
                    layernorm()
                    masks(5, 6, 7)
                else:
                    layernorm()
                    masks(5)
                    elu(elu_half)
                    masks(6)
                    elu(elu_rest)
                    masks(7)

            def last():
                for k, w in enumerate(tiles_in):
                    lo = k * NB
                    copy_acc(LAST, 1, k)
                    dve.wait_ge(acc_copied, NB * LAST + k + 1)
                    nc.vector.reciprocal(rec[:, lo:lo + w],
                                         accs[:, lo:lo + w, D]).then_inc(last_rec, 1)
                    dve.wait_ge(last_rec, k + 1)
                    x = x3_at(x1, B - 1)
                    for t in range(lo, lo + w):
                        op = nc.vector.scalar_tensor_tensor(x[:, t, :], accs[:, t, 0:D],
                                                            rec[:, t:t + 1], x[:, t, :],
                                                            ALU.mult, ALU.add)
                    op.then_inc(last_ready, 1)

            schedule(dve, stage, setup, last)

        @block.tensor
        def _(pe):
            def transposes(m):
                if isinstance(m, int) and m == 1:
                    pe.wait_ge(row0_dve, 1)
                    pe.wait_ge(row0_ready, 1)
                elif not isinstance(m, int) or m > 1:
                    pe.wait_ge(rT_ready, m - 1)
                if not (isinstance(m, int) and m == 0):
                    pe.wait_ge(xn_ready, xn_before(m + 1))
                for t in [*range(DVE_SHARE, T), *range(DVE_SHARE)]:
                    if isinstance(m, int) and m == 0 and t < DVE_SHARE:
                        pe.wait_ge(xn_dve, t + 1)
                    elif isinstance(m, int) and m == 0:
                        pe.wait_ge(xn_ready, t - DVE_SHARE + 1)
                    mm = nc.tensor.transpose(tp[:, t * P:(t + 1) * P], xn[:, t, :], ident[:, :])
                mm.then_inc(tr_done, 1)

            def project(m, l):
                pe.wait_ge(hT_ready, m + 1)
                if not isinstance(m, int) or m > 0:
                    pe.wait_ge(wh_ready, T * m)
                for t, (k, s) in enumerate(bank_of):
                    nc.tensor.matmul(prj[:, k, s * E:(s + 1) * E], hT[:, t * P:(t + 1) * P],
                                     w_ext[:, l, :], start=(s == 0), stop=True,
                                     skip_group_check=True)
                nc.tensor.matmul(USUM, hsum[:, 0:1].to_broadcast([P, P]), w_ext[:, l, 0:D],
                                 start=False, stop=True, skip_group_check=True).then_inc(prj_done, 1)

            def spread_emax(m):
                pe.wait_ge(emax_ready, m + 1)
                nc.tensor.transpose(tp[:, 0:P], emax[:, 0:1].to_broadcast([P, P]),
                                    ident[:, :]).then_inc(emax_spread, 1)

            def spread_r(g):
                pe.wait_ge(sqr_ready, 1)
                for t in range(T):
                    mm = nc.tensor.transpose(tp[:, t * P:(t + 1) * P],
                                             sqr[:, g, 2, t:t + 1].to_broadcast([P, P]), ident[:, :])
                    if t % 4 == 3:
                        mm.then_inc(r_spread, 1)

            def turn_r(m, g):
                pe.wait_ge(sqr_ready, m + 1)
                nc.tensor.transpose(tp[0:T, 0:P], sqr[:, g, 2, :],
                                    ident[:, :]).then_inc(r_turned, 1)

            def keep_warm(count):
                for _ in range(count):
                    nc.tensor.transpose(acc[:, 0, 0:P], ident[:, :], ident[:, :])

            def attend(n, g, t):
                if t % 4 == 0:
                    pe.wait_ge(wh_ready, T * n + t + 4)
                halved = first(n) and t == 0
                if halved:
                    pe.wait_ge(p_half, 1)
                else:
                    pe.wait_ge(p_ready, T * n + t + 1)
                for i, (k, s) in enumerate(bank_of):
                    if halved and i == T // 2:
                        pe.wait_ge(p_ready, 1)
                    if t == 0 and s == 0 and not (isinstance(n, int) and n == 0):
                        pe.wait_ge(acc_copied, NB * (n - 1) + k + 1)
                    mm = nc.tensor.matmul(acc[:, k, s * C:(s + 1) * C],
                                          pbuf[:, t, i * P:(i + 1) * P], wh[:, g, t, :],
                                          start=(t == 0 and s == 0), stop=(t == T - 1),
                                          skip_group_check=True)
                    if t == T - 1 and s == tiles_in[k] - 1:
                        mm.then_inc(acc_done, 1)
                if t == TAKE_AFTER:
                    mm.then_inc(p_used, 1)

            def attend_last(n, g):
                pe.wait_ge(wh_ready, T * n + T)
                for k, w in enumerate(tiles_in):
                    for t in range(LAST_SPLIT, T):
                        if k == 0:
                            pe.wait_ge(p_ready, T * n + t + 1)
                        for s in range(w):
                            i = k * NB + s
                            mm = nc.tensor.matmul(acc[:, k, s * C:(s + 1) * C],
                                                  pbuf[:, t, i * P:(i + 1) * P], wh[:, g, t, :],
                                                  start=False, stop=(t == T - 1),
                                                  skip_group_check=True)
                    mm.then_inc(acc_done, 1)

            def setup():
                pe.wait_ge(const_set, 5)
                keep_warm(WARM[0])
                pe.wait_ge(w_in, 96)
                for l in range(2):
                    mm = nc.tensor.matmul(prj[:, 0, 2 * l:2 * l + 2], w_tr[:, l, :], a_cols[:, l, :],
                                          start=(l == 0), stop=True, skip_group_check=True)
                mm.then_inc(wa_done, 1)
                keep_warm(WARM[1])
                transposes(0)
                keep_warm(WARM[2])
                pe.wait_ge(wext_ready, 1)
                project(0, 0)
                keep_warm(WARM[3])
                spread_emax(0)
                keep_warm(WARM[4])
                spread_r(0)
                transposes(1)

            def stage(n, g, l, b, epi, prep, norm):
                def tiles(*ts):
                    for t in ts:
                        attend(n, g, t)

                if first(n):
                    tiles(0)
                    project(1, prep)
                    tiles(1)
                    spread_emax(1)
                    tiles(2)
                    turn_r(1, 1)
                    tiles(3, 4, 5, 6)
                    transposes(2)
                    tiles(7)
                elif isinstance(n, int) and n == LAST:
                    tiles(*range(LAST_SPLIT))
                    attend_last(n, g)
                else:
                    project(n + 1, prep)
                    tiles(0)
                    spread_emax(n + 1)
                    tiles(1)
                    turn_r(n + 1, 1 - g)
                    tiles(2, 3, 4, 5, 6)
                    if norm is not None:
                        transposes(n + 2)
                    tiles(7)

            schedule(pe, stage, setup, lambda: None)


def kernel(x, adj, L0_gnn_W, L0_gnn_a, L1_gnn_W, L1_gnn_a):
    import numpy as np
    import concourse.bacc as bacc
    from concourse.bass_utils import run_bass_kernel_spmd

    x = np.ascontiguousarray(x)
    b, n, d = x.shape
    t = n // P
    adj = np.asarray(adj).reshape(b, P, t, P, t).transpose(0, 4, 3, 2, 1).reshape(b, t, P, n)
    w0, w1 = np.asarray(L0_gnn_W), np.asarray(L1_gnn_W)
    ins = {
        "x": x, "adj": adj,
        "w0": w0, "w0t": w0.T, "a0": np.asarray(L0_gnn_a).reshape(2, d).T,
        "w1": w1.T, "w1t": w1, "a1": np.asarray(L1_gnn_a).reshape(2, d).T,
    }
    nc = bacc.Bacc("TRN2", target_bir_lowering=False, num_devices=1)
    arrays, aps = {}, []
    for name, a in ins.items():
        a = np.ascontiguousarray(a)
        arrays[f"in_{name}"] = a
        aps.append(nc.dram_tensor(f"in_{name}", a.shape, mybir.dt.from_np(a.dtype),
                                  kind="ExternalInput").ap())
    r_rows = nc.dram_tensor("r_rows", (t, P), F32, kind="Internal").ap()
    res = nc.dram_tensor("out_x", x.shape, F32, kind="ExternalOutput").ap()
    gat_two_layers(nc, *aps, r_rows, res)
    r = run_bass_kernel_spmd(nc, [arrays], core_ids=[0])
    return r.results[0]["out_x"]
```
